# Optimizing a Trainium2 kernel written in Bass

```python
import numpy as np
import jax
import jax.numpy as jnp

def _softmax(x, axis=-1):
    return jax.nn.softmax(x, axis=axis)

def _gelu(x):
    return jax.nn.gelu(x, approximate=True)

def _silu(x):
    return jax.nn.silu(x)

def _sigmoid(x):
    return jax.nn.sigmoid(x)

def _layernorm(x, axis=-1, eps=1e-05):
    m = jnp.mean(x, axis=axis, keepdims=True)
    v = jnp.var(x, axis=axis, keepdims=True)
    return (x - m) / jnp.sqrt(v + eps)

def _scatter_add(tgt, idx, src, axis=0):
    return tgt.at[idx].add(src)

def _segment_sum(src, seg, n):
    return jax.ops.segment_sum(src, seg, n)
kernel_name = 'mk_adj_preln_d1_adj_r2_ec2c25'

def setup_inputs(seed: int=0):
    np.random.seed(seed)
    _w = jnp.asarray

    def _rec_inputs():
        import jax
        import jax.numpy as jnp
        _gk = jax.random.key(seed)
        x = 7.22e-05 + 1 * jax.random.normal(jax.random.fold_in(_gk, 1), (32, 256, 1024), jnp.float32)
        _w = (1.0 + jnp.arange(256, dtype=jnp.float32)) ** (-0.5)
        _w = _w / _w.mean()
        _pij = jnp.clip(0.03125 * _w[:, None] * _w[None, :], 0.0, 1.0)
        _a = jax.random.uniform(jax.random.fold_in(_gk, 2), (256, 256)) < _pij
        _a = jnp.logical_or(_a, jnp.swapaxes(_a, -1, -2))
        _a = jnp.logical_or(_a, jnp.eye(256, dtype=bool))
        _af = _a.astype(jnp.float32)
        _af = _af * jax.random.uniform(jax.random.fold_in(_gk, 3), (256, 256), jnp.float32, 0.05, 0.0885215)
        adj = _af
        return (x, adj)
    x, adj = _rec_inputs()

    def _L0_gnn_setup():
        import jax, jax.numpy as jnp
        import numpy as np
        B, S, N = (8, 256, 1024)
        HID = 256
        K = 8

        def _construct_adj(x, k):
            Bn, Sn, Nn = x.shape
            fv = x.mean(axis=1)
            nf = fv / jnp.linalg.norm(fv, axis=1, keepdims=True)
            sim = nf[:, :, None] * nf[:, None, :]
            kk = min(k, Nn - 1)
            _, idx = jax.lax.top_k(sim, kk + 1)
            idx = idx[..., 1:]
            b_ix = jnp.arange(Bn)[:, None, None]
            r_ix = jnp.arange(Nn)[None, :, None]
            adj = jnp.zeros((Bn, Nn, Nn), x.dtype).at[b_ix, r_ix, idx].set(1.0)
            adj = jnp.maximum(adj, jnp.swapaxes(adj, 1, 2))
            d = jnp.arange(Nn)
            adj = adj.at[:, d, d].set(1.0)
            return adj

        def _gc(x, adj, W, b):
            deg = adj.sum(axis=2, keepdims=True)
            deg = jnp.where(deg == 0, jnp.ones_like(deg), deg)
            h = x @ W.T + b
            return jnp.einsum('bij,bjh->bih', adj / deg, h)
        key = jax.random.key(seed)
        k0, k1, k2 = jax.random.split(key, 3)
        x = jax.random.normal(k0, (B, S, N), jnp.float32)
        W1 = jax.random.normal(k1, (HID, S), jnp.float32) * 0.02
        b1 = jnp.zeros((HID,), jnp.float32)
        W2 = jax.random.normal(k2, (S, HID), jnp.float32) * 0.02
        b2 = jnp.zeros((S,), jnp.float32)
        return {'x': x, 'W1': W1, 'b1': b1, 'W2': W2, 'b2': b2}
    _L0_gnn_all = _L0_gnn_setup()
    _L0_gnn_in = {k: v for k, v in _L0_gnn_all.items() if k in ('b1', 'b2')}
    del _L0_gnn_all
    return {'x': x, 'adj': adj, 'L0_gnn_b1': _L0_gnn_in['b1'], 'L0_gnn_b2': _L0_gnn_in['b2']}

def reference(x, adj, L0_gnn_b1, L0_gnn_b2):
    import jax
    import jax.numpy as jnp

    def _L0_gnn_ref(x, W1, b1, W2, b2):
        import jax, jax.numpy as jnp
        import numpy as np
        B, S, N = (8, 256, 1024)
        HID = 256
        K = 8

        def _construct_adj(x, k):
            Bn, Sn, Nn = x.shape
            fv = x.mean(axis=1)
            nf = fv / jnp.linalg.norm(fv, axis=1, keepdims=True)
            sim = nf[:, :, None] * nf[:, None, :]
            kk = min(k, Nn - 1)
            _, idx = jax.lax.top_k(sim, kk + 1)
            idx = idx[..., 1:]
            b_ix = jnp.arange(Bn)[:, None, None]
            r_ix = jnp.arange(Nn)[None, :, None]
            adj = jnp.zeros((Bn, Nn, Nn), x.dtype).at[b_ix, r_ix, idx].set(1.0)
            adj = jnp.maximum(adj, jnp.swapaxes(adj, 1, 2))
            d = jnp.arange(Nn)
            adj = adj.at[:, d, d].set(1.0)
            return adj

        def _gc(x, adj, W, b):
            deg = adj.sum(axis=2, keepdims=True)
            deg = jnp.where(deg == 0, jnp.ones_like(deg), deg)
            h = x @ W.T + b
            return jnp.einsum('bij,bjh->bih', adj / deg, h)
        adj = _construct_adj(x, K)
        xr = jnp.swapaxes(x, 1, 2)
        h = jax.nn.relu(_gc(xr, adj, W1, b1))
        h = _gc(h, adj, W2, b2)
        return jnp.swapaxes(h, 1, 2)
    h = jnp.maximum(_layernorm(x, axis=-1), 0.0)
    x = x + _L0_gnn_ref(h, adj, L0_gnn_b1, adj, L0_gnn_b2)
    return x

_drawn_inputs = setup_inputs


def setup_inputs(seed=0):
    import zlib

    import numpy as np

    out = dict(_drawn_inputs(seed))
    spreads = {'L0_gnn_b1': (0.0, 0.403), 'L0_gnn_b2': (0.0, 0.1)}
    factors = {}
    for name, (base, spread) in spreads.items():
        noise = np.random.default_rng([zlib.crc32(name.encode()), seed]).standard_normal(out[name].shape)
        drawn = base * np.exp(spread * noise) if base else spread * noise
        out[name] = jnp.asarray(drawn.astype(out[name].dtype))
    for name, factor in factors.items():
        out[name] = (out[name] * factor).astype(out[name].dtype)
    return out
```

```python
import concourse.bass as bass
from concourse import mybir
from contextlib import ExitStack


def adjacency_gnn_kernel(nc, x, adj, b1, b2, out):
    F32 = mybir.dt.float32
    F16 = mybir.dt.float16
    U32 = mybir.dt.uint32
    I32 = mybir.dt.int32
    ALU = mybir.AluOpType
    ACT = mybir.ActivationFunctionType
    AX = mybir.AxisListType

    B, S, N = x.shape
    P = 128
    KT = S // P
    HALF = 512
    NH = N // HALF
    GB = 4
    NG = B // GB
    SLOTS = 2 * GB
    T = 8
    C = T + 1
    DEG = float(T + 1)
    HS = 1024.0
    EPS = 1e-5
    TINY = 2.0 ** -60

    ctx = ExitStack()
    with ctx:
        def sb(name, shape, dt=F32):
            return ctx.enter_context(nc.sbuf_tensor(name, shape, dt))

        def sem(name):
            return ctx.enter_context(nc.semaphore(name))

        x_sb = sb("x_sb", [P, SLOTS, KT, N])
        h_split = sb("h_split", [P, SLOTS, 2, KT, N], F16)
        h_f32 = sb("h_f32", [P, 2, KT, N])
        g_f32 = sb("g_f32", [P, 2, KT, N])
        g_split = sb("g_split", [P, 2, 2, KT, N], F16)
        adj_sb = sb("adj_sb", [P, KT, S])
        w_part = sb("w_part", [P, 2, KT, S], F16)
        w_t = sb("w_t", [P, 2, KT, S], F16)
        ident = sb("ident", [P, P], F16)
        onehot = sb("onehot", [P, 2 * 32], F16)
        eps_t = sb("eps_t", [P, 1])
        b1_t = sb("b1_t", [P, KT])
        b2_t = sb("b2_t", [P, KT])
        setup = sb("setup", [P, 24, KT])
        sc1 = sb("sc1", [P, KT, 2])
        b1p = sb("b1p", [P, KT, 2])
        sc2 = sb("sc2", [P, KT])
        sc2T = sb("sc2T", [P, KT])
        stats = sb("stats", [P, 2, KT, NH, 6])
        meanvar = sb("meanvar", [P, 2, KT, 2])
        std = sb("std", [P, 2, KT])
        nrm = sb("nrm", [P, 5, KT])
        rstd = sb("rstd", [P, 2, KT])
        nmr = sb("nmr", [P, 2, KT])
        h_sum = sb("h_sum", [P, SLOTS, KT])
        g_sum = sb("g_sum", [P, 2, KT])
        fv = sb("fv", [GB, N])
        fv_rest = sb("fv_rest", [GB, N])
        top8 = sb("top8", [GB, 8])
        next8 = sb("next8", [GB, 8])
        rank_idx = sb("rank_idx", [GB, 2, 20], U32)
        fv_min = sb("fv_min", [GB, NG, NH])
        mv_in = sb("mv_in", [P, KT, GB, 2 * C], F16)
        mv_sum = sb("mv_sum", [P, KT, GB, C])
        hub_sum = sb("hub_sum", [P, KT, GB, 2])
        bq = sb("bq", [P, 2, KT, GB, 2])
        gt = sb("gt", [P, KT, GB, T])
        gt_sum = sb("gt_sum", [P, KT, GB])
        d_sum = sb("d_sum", [P, 2, KT, GB])
        q8 = sb("q8", [P, 2, KT, GB])
        q_split = sb("q_split", [P, KT, 2, GB], F16)
        wq = sb("wq", [P, KT, GB])
        bias2 = sb("bias2", [P, 2, KT, GB])
        u2 = sb("u2", [P, 2, KT])
        u_split = sb("u_split", [P, 2, KT, 1], F16)

        ps1 = [ctx.enter_context(nc.psum_tensor(f"ps1_{m}", [P, NH, HALF], F32)) for m in range(KT)]
        ps2 = [ctx.enter_context(nc.psum_tensor(f"ps2_{u}", [P, HALF], F32)) for u in range(2)]
        ps_cs = ctx.enter_context(nc.psum_tensor("ps_cs", [P, HALF], F32))
        ps_mv = ctx.enter_context(nc.psum_tensor("ps_mv", [P, HALF], F32))
        mv1 = ps_mv[:, 0:KT * GB * 2 * C].rearrange("p (m i l j) -> p m i l j", m=KT, i=GB, l=2)
        mv2 = ps_mv[:, 256:256 + KT * 2 * GB].rearrange("p (m l i) -> p m l i", m=KT, l=2)

        consts = sem("consts")
        in_small = sem("in_small")
        setup_dve = sem("setup_dve")
        setup_pool = sem("setup_pool")
        w_split_ready = sem("w_split_ready")
        w_transposed = sem("w_transposed")
        w_ready = sem("w_ready")
        x_in = [[sem(f"x_in{s}_{k}") for k in range(KT)] for s in range(SLOTS)]
        stored = [[sem(f"stored{s}_{k}") for k in range(KT)] for s in range(2)]
        s_chain = sem("dve_chain")
        s_var = sem("var_ready")
        s_std = sem("std_ready")
        s_norm = sem("norm_ready")
        s_h = sem("h_ready")
        s_hhi = sem("h_hi_ready")
        s_hlo = sem("h_lo_ready")
        s_cs = sem("colsum_done")
        s_csread = sem("colsum_read")
        s_rank = sem("hubs_ranked")
        s_hubs = sem("hubs_gathered")
        s_mv1 = sem("matvec1_done")
        s_q = sem("q_ready")
        s_bias1 = sem("bias1_ready")
        s_mv2 = sem("matvec2_done")
        s_bias2 = sem("bias2_ready")
        s_gemm1 = sem("gemm1_done")
        s_g = sem("g_ready")
        s_ghi = sem("g_hi_ready")
        s_glo = sem("g_lo_ready")
        s_hubset = sem("hub_columns_set")
        s_gemm2 = sem("gemm2_done")
        s_xb = sem("x_with_bias2")
        s_o = sem("out_ready")

        UN = KT * NH

        def ge(eng, s, v):
            if not isinstance(v, int) or v > 0:
                eng.wait_ge(s, v)

        class At:
            def __init__(self, r, p, i):
                self.i, self.p = i, p
                self.n = 2 * GB * r + GB * p + i
                self.G = 2 * r + p
                self.r = r
                self.slot = GB * p + i
                self.par = i % 2

        def ahead(r, p, i, d):
            t = GB * p + i + d
            a = At(r + t // SLOTS, t % SLOTS // GB, t % GB)
            return a if not isinstance(a.n, int) or 0 <= a.n < B else None

        def run_groups(eng, steps):
            steps(0, 0)
            with eng.Fori(0, NG // 2 - 2) as r:
                steps(r, 1)
                steps(r + 1, 0)
            for r, p in ((NG // 2 - 2, 1), (NG // 2 - 1, 0), (NG // 2 - 1, 1)):
                steps(r, p)

        def nxt(r, p):
            q = (r, 1) if p == 0 else (r + 1, 0)
            return None if isinstance(r, int) and q[0] == NG // 2 else q

        LEAD = 5

        def hub_columns(eng, regs, a):
            eng.load(regs, rank_idx[a.i:a.i + 1, a.p, 4:4 + T])
            return [eng.snap(g, min_val=0, max_val=N - 1) for g in regs]

        def gather_hubs(eng, ops, regs, a):
            for t, v in enumerate(hub_columns(eng, regs, a)):
                ins = ops.tensor_copy(
                    mv_in[:, :, a.i, :].rearrange("p k (l j) -> p l k j", l=2)[:, :, :, t:t + 1],
                    h_split[:, a.slot, :, :, bass.ds(v, 1)])
            return ins

        DVE_GATHERS = 1

        block = ctx.enter_context(nc.Block())

        @block.sync
        def _(sp):
            def load(slot, n, k):
                sp.dma_start(x_sb[:, slot, k], x[bass.ds(n, 1), k * P:(k + 1) * P, :].rearrange("a p n -> p (a n)")
                             ).then_inc(x_in[slot][k], 16)

            for k in range(KT):
                load(0, 0, k)
            sp.dma_start(adj_sb[:, :, :], adj.rearrange("(m p) s -> p m s", p=P)).then_inc(in_small, 16)
            sp.dma_start(b1_t[:, :], b1.rearrange("(m p) -> p m", p=P),
                         allow_slow_non_contiguous=True).then_inc(in_small, 16)
            sp.dma_start(b2_t[:, :], b2.rearrange("(m p) -> p m", p=P),
                         allow_slow_non_contiguous=True).then_inc(in_small, 16)
            for s in range(1, SLOTS):
                for k in range(KT):
                    load(s, s, k)

            def store(a, reload):
                for m in range(KT):
                    sp.wait_ge(s_o, UN * a.n + NH * (m + 1))
                    dst = out[bass.ds(a.n, 1), m * P:(m + 1) * P, :].rearrange("a p n -> p (a n)")
                    sp.dma_start(dst, g_f32[:, a.par, m]).then_inc(stored[a.par][m], 16)
                    if reload:
                        load(a.slot, a.n + SLOTS, m)

            def steps(r, p):
                for i in range(GB):
                    a = ahead(r, p, i, -1)
                    if a:
                        store(a, not isinstance(a.n, int) or a.n + SLOTS < B)

            run_groups(sp, steps)
            store(At(NG // 2 - 1, 1, GB - 1), False)
            for s in range(2):
                for m in range(KT):
                    sp.wait_ge(stored[s][m], 16 * (B // 2))

        @block.gpsimd
        def _(pool):
            pool.memset(ident[:, :], 0.0).then_inc(setup_pool, 1)
            pool.memset(onehot[:, :], 0.0).then_inc(setup_pool, 1)
            pool.memset(eps_t[:, :], EPS).then_inc(consts, 1)
            pool.wait_ge(setup_pool, 2)
            pool.affine_select(out=ident[:, :], in_=ident[:, :], compare_op=ALU.not_equal, fill=1.0,
                               base=0, pattern=[[-1, P]], channel_multiplier=1).then_inc(consts, 1)
            pool.memset(onehot[:, 32:33], 1.0).then_inc(consts, 1)

            def h_low(a):
                for k in range(KT):
                    pool.wait_ge(s_hhi, KT * a.n + k + 1)
                    pool.tensor_tensor(h_split[:, a.slot, 1, k], h_f32[:, a.par, k],
                                       h_split[:, a.slot, 0, k], ALU.subtract).then_inc(s_hlo, 1)

            def g_low(a):
                for m in range(KT if a.i else KT - 1):
                    pool.wait_ge(s_ghi, KT * a.n + m + 1)
                    pool.tensor_tensor(g_split[:, a.par, 1, m], g_f32[:, a.par, m],
                                       g_split[:, a.par, 0, m], ALU.subtract).then_inc(s_glo, 1)

            pool.wait_ge(setup_dve, 1)
            pool.partition_all_reduce(setup[:, 11, 0:1], setup[:, 10, 0:1], P, bass.bass_isa.ReduceOp.max
                                      ).then_inc(setup_pool, 1)
            for d in range(LEAD):
                h_low(ahead(0, 0, 0, d))

            regs = [pool.alloc_register(f"pool_hub{t}") for t in range(T)]

            def gather(r, p, count):
                pool.wait_ge(consts, 3)
                pool.wait_ge(s_rank, count)
                for i in range(DVE_GATHERS, GB):
                    ins = gather_hubs(pool, pool, regs, At(r, p, i))
                ins.then_inc(s_hubs, 1)

            gather(0, 0, 1)

            def steps(r, p):
                for i in range(GB):
                    q = nxt(r, p) if i == GB - 1 else None
                    if q:
                        count = 2 * q[0] + q[1] + 1
                        count = count if isinstance(count, int) else pool.snap(count)
                        pool.wait_ge(s_csread, count)
                    if b := ahead(r, p, i, LEAD):
                        h_low(b)
                    g_low(At(r, p, i))
                    if q:
                        gather(*q, count)

            run_groups(pool, steps)

        @block.scalar
        def _(act):
            act.wait_ge(consts, 3)

            def std_dev(a):
                act.wait_ge(s_var, a.n + 1)
                nc.scalar.activation(std[:, a.par], meanvar[:, a.par, :, 1], ACT.Sqrt, bias=eps_t[:, 0:1]
                                     ).then_inc(s_std, 1)

            def h_tiles(a):
                act.wait_ge(s_norm, a.n + 1)
                for k in range(KT):
                    ge(act, s_hlo, KT * (a.n - 2) + k + 1)
                    nc.scalar.activation(h_f32[:, a.par, k], x_sb[:, a.slot, k], ACT.Relu,
                                         bias=nmr[:, a.par, k:k + 1], scale=rstd[:, a.par, k:k + 1],
                                         accum_out=h_sum[:, a.slot, k:k + 1]).then_inc(s_h, 1)
                for k in range(KT):
                    act.wait_ge(s_h, KT * a.n + k + 1)
                    nc.scalar.activation(h_split[:, a.slot, 0, k], h_f32[:, a.par, k], ACT.Copy
                                         ).then_inc(s_hhi, 1)

            def add_bias2(a):
                act.wait_ge(s_bias2, a.G + 1)
                for m in range(KT):
                    nc.scalar.activation(x_sb[:, a.slot, m], x_sb[:, a.slot, m], ACT.Identity,
                                         bias=bias2[:, a.p, m, a.i:a.i + 1]).then_inc(s_xb, 1)

            def g_tiles(a):
                act.wait_ge(s_bias1, a.G + 1)
                for m in range(KT):
                    act.wait_ge(s_gemm1, KT * a.n + m + 1)
                    ge(act, stored[a.par][m], 16 * (a.n // 2 if isinstance(a.n, int) else
                                                    GB * a.r + (GB * a.p + a.i) // 2))
                    if m == 0:
                        ge(act, s_hubset, a.n - 1)
                    nc.scalar.activation(g_f32[:, a.par, m], ps1[m][:, :, :].rearrange("p a n -> p (a n)"),
                                         ACT.Relu, bias=bq[:, a.p, m, a.i, 0:1], scale=sc1[:, m, 0:1],
                                         accum_out=g_sum[:, a.par, m:m + 1]).then_inc(s_g, 1)
                ge(act, s_gemm2, UN * (a.n - 1))
                for m in range(KT):
                    act.wait_ge(s_g, KT * a.n + m + 1)
                    nc.scalar.activation(g_split[:, a.par, 0, m], g_f32[:, a.par, m], ACT.Copy
                                         ).then_inc(s_ghi, 1)

            for d in range(LEAD):
                std_dev(ahead(0, 0, 0, d))
                h_tiles(ahead(0, 0, 0, d))

            std_dev(ahead(0, 0, 0, LEAD))

            def steps(r, p):
                for i in range(GB):
                    if b := ahead(r, p, i, LEAD):
                        h_tiles(b)
                    if b := ahead(r, p, i, -1):
                        add_bias2(b)
                    g_tiles(At(r, p, i))
                    if b := ahead(r, p, i, LEAD + 1):
                        std_dev(b)

            run_groups(act, steps)
            add_bias2(At(NG // 2 - 1, 1, GB - 1))

        @block.vector
        def _(dve):
            ch = [0]
            V = nc.vector

            def link(ins):
                ins.then_inc(s_chain, 1)
                ch[0] += 1
                dve.wait_ge(s_chain, ch[0])

            dve.wait_ge(in_small, 48)
            ROWMAX, ROWSUM, CPOW, CINV, BND, BPOW, PINV, PSC, ALPHA, PB = range(10)
            st = lambda j: setup[:, j, :]
            link(V.tensor_reduce(st(ROWMAX), adj_sb[:, :, :], AX.X, ALU.max, apply_absolute_value=True))
            link(V.tensor_reduce(st(ROWSUM), adj_sb[:, :, :], AX.X, ALU.add, apply_absolute_value=True))
            link(V.tensor_scalar(st(ROWMAX), st(ROWMAX), TINY, None, ALU.max))
            link(V.tensor_scalar(st(CPOW).bitcast(I32), st(ROWMAX).bitcast(I32), 0x7F800000, None,
                                 ALU.bitwise_and))
            link(V.reciprocal(st(CINV), st(CPOW)))
            link(V.tensor_scalar(st(CINV), st(CINV), 2.0 ** 13, None, ALU.mult))
            for m in range(KT):
                link(V.tensor_scalar(adj_sb[:, m], adj_sb[:, m], setup[:, CINV, m:m + 1], None, ALU.mult))
            link(V.tensor_copy(w_part[:, 0], adj_sb[:, :, :]))
            link(V.tensor_tensor(w_part[:, 1], adj_sb[:, :, :], w_part[:, 0], ALU.subtract))
            V.tensor_scalar(st(BND), b1_t[:, :], 0.0, None, ALU.add).then_inc(w_split_ready, 1)
            dve.wait_ge(w_split_ready, 1)
            link(V.tensor_reduce(setup[:, BND, :].rearrange("p (m o) -> p m o", o=1),
                                 b1_t[:, :].rearrange("p (m o) -> p m o", o=1), AX.X, ALU.max,
                                 apply_absolute_value=True))
            link(V.scalar_tensor_tensor(st(BND), st(ROWSUM), 32.0, st(BND), ALU.mult, ALU.add))
            link(V.tensor_reduce(setup[:, 10, 0:1], st(BND), AX.X, ALU.max))
            link(V.tensor_scalar(setup[:, 10, 0:1], setup[:, 10, 0:1], TINY, None, ALU.max))
            V.tensor_copy(setup[:, 12, 0:1], setup[:, 10, 0:1]).then_inc(setup_dve, 1)
            dve.wait_ge(setup_pool, 3)
            link(V.tensor_scalar(setup[:, BPOW, 0:1].bitcast(I32), setup[:, 11, 0:1].bitcast(I32),
                                 0x7F800000, None, ALU.bitwise_and))
            link(V.reciprocal(setup[:, PSC, 0:1], setup[:, BPOW, 0:1]))
            link(V.tensor_scalar(setup[:, PSC, 0:1], setup[:, PSC, 0:1], 2.0 ** 11, None, ALU.mult))
            link(V.tensor_scalar(setup[:, PINV, 0:1], setup[:, BPOW, 0:1], 2.0 ** -11, None, ALU.mult))
            psc, pinv = setup[:, PSC, 0:1], setup[:, PINV, 0:1]
            link(V.tensor_scalar(sc1[:, :, 1], st(CPOW), 2.0 ** -13 / HS, psc, ALU.mult, ALU.mult))
            link(V.tensor_scalar(sc1[:, :, 0], sc1[:, :, 1], 1.0 / DEG, None, ALU.mult))
            link(V.tensor_scalar(sc2[:, :], st(CPOW), 2.0 ** -13 / DEG, pinv, ALU.mult, ALU.mult))
            link(V.tensor_scalar(sc2T[:, :], sc2[:, :], float(T), None, ALU.mult))
            for c in range(2):
                link(V.tensor_scalar(b1p[:, :, c], b1_t[:, :], psc, None, ALU.mult))
            dve.wait_ge(w_transposed, 1)
            for w in range(2):
                for m in range(KT):
                    ins = V.tensor_copy(w_t[:, w, :, m * P:(m + 1) * P],
                                        ps1[m][:, w].bitcast(F16)[:, 0:KT * P].rearrange("p (k o) -> p k o", k=KT))
            ins.then_inc(w_ready, 1)

            def bn(a, c):
                for k in range(KT):
                    dve.wait_ge(x_in[a.slot][k], 16 * (a.r + 1))
                    for hf in range(NH):
                        ins = V.bn_stats(stats[:, a.par, k, hf], x_sb[:, a.slot, k, hf * HALF:(hf + 1) * HALF])
                c.link(ins)
                for k in range(KT):
                    ins = V.bn_aggr(meanvar[:, a.par, k], stats[:, a.par, k].rearrange("p h s -> p (h s)"))
                ins.then_inc(s_var, 1)

            def norm(a, c):
                mean, var = meanvar[:, a.par, :, 0], meanvar[:, a.par, :, 1]
                y0, ve, ysq, t1, t2 = (nrm[:, z] for z in range(5))
                dve.wait_ge(s_std, a.n + 1)
                V.reciprocal(y0, std[:, a.par])
                c.link(V.tensor_scalar(ve, var, EPS, None, ALU.add))
                c.link(V.tensor_tensor(ysq, y0, y0, ALU.mult))
                c.link(V.tensor_tensor(t1, ysq, ve, ALU.mult))
                c.link(V.tensor_scalar(t2, t1, -0.5, 1.5, ALU.mult, ALU.add))
                c.link(V.scalar_tensor_tensor(rstd[:, a.par], y0, HS, t2, ALU.mult, ALU.mult))
                V.scalar_tensor_tensor(nmr[:, a.par], mean, -1.0, rstd[:, a.par], ALU.mult, ALU.mult
                                       ).then_inc(s_norm, 1)

            def rank_top(r, p, c):
                G = 2 * r + p
                dve.wait_ge(s_cs, GB * (G + 1))
                for hf in range(NH):
                    ins = V.tensor_scalar(fv[:, hf * HALF:(hf + 1) * HALF], ps_cs[32 * hf:32 * hf + GB, :],
                                          0.0, None, ALU.add)
                ins.then_inc(s_csread, 1)
                dve.wait_ge(consts, 3)
                dve.wait_ge(s_csread, G + 1)
                idx = rank_idx[:, p]
                c.link(V.max(top8[:, :], fv[:, :]))

            def rank_index(r, p, c):
                idx = rank_idx[:, p]
                V.max_index(idx[:, 3:11], top8[:, :], fv[:, :])
                c.link(V.match_replace(fv_rest[:, :], top8[:, :], fv[:, :], -1.0))

            def rank_next(r, p, c):
                idx = rank_idx[:, p]
                c.link(V.max(next8[:, :], fv_rest[:, :]))
                V.max_index(idx[:, 11:19], next8[:, :], fv_rest[:, :]).then_inc(s_rank, 1)

            regs = [dve.alloc_register(f"hub{t}") for t in range(T)]

            def gather(r, p):
                count = 2 * r + p + 1
                count = count if isinstance(count, int) else dve.snap(count)
                dve.wait_ge(consts, 3)
                dve.wait_ge(s_rank, count)
                for i in range(DVE_GATHERS):
                    ins = gather_hubs(dve, V, regs, At(r, p, i))
                ins.then_inc(s_hubs, 1)

            def means(r, p, c):
                G = 2 * r + p
                dve.wait_ge(s_hlo, KT * (At(r, p, 0).n + GB))
                ge(dve, s_mv1, G)
                sums = h_sum[:, GB * p:GB * (p + 1), :].rearrange("p i k -> p k i")
                c.link(V.tensor_scalar(mv_in[:, :, :, T], sums, 1.0 / N, None, ALU.mult))
                c.link(V.scalar_tensor_tensor(mv_in[:, :, :, C + T], sums, 1.0 / N, mv_in[:, :, :, T],
                                              ALU.mult, ALU.subtract))

            def bias1_chain(r, p, c):
                G = 2 * r + p
                dve.wait_ge(s_mv1, G + 1)
                for m in range(KT):
                    ins = V.tensor_reduce(mv_sum[:, m], mv1[:, m].rearrange("p i l j -> p i j l"), AX.X, ALU.add)
                c.link(ins)
                V.tensor_copy(hub_sum[:, :, :, 1], mv_sum[:, :, :, T])
                c.link(V.tensor_reduce(hub_sum[:, :, :, 0], mv_sum[:, :, :, 0:T], AX.X, ALU.add))
                for m in range(KT):
                    ins = V.tensor_tensor(hub_sum[:, m], hub_sum[:, m],
                                          sc1[:, m:m + 1, :].to_broadcast([P, GB, 2]), ALU.mult)
                c.link(ins)
                for m in range(KT):
                    ins = V.tensor_tensor(bq[:, p, m], hub_sum[:, m],
                                          b1p[:, m:m + 1, :].to_broadcast([P, GB, 2]), ALU.add)
                ins.then_inc(s_bias1, 1)

            def q_chain(r, p, c):
                G = 2 * r + p
                dve.wait_ge(s_bias1, G + 1)
                c.link(V.tensor_scalar(bq[:, p, :, :, 1], bq[:, p, :, :, 1], 0.0, None, ALU.max))
                for m in range(KT):
                    ins = V.tensor_scalar(gt[:, m], mv_sum[:, m, :, 0:T], sc1[:, m, 0:1], None, ALU.mult)
                c.link(ins)
                for m in range(KT):
                    V.tensor_tensor(gt[:, m], gt[:, m], bq[:, p, m, :, 0:1].to_broadcast([P, GB, T]), ALU.add)
                V.tensor_copy(q_split[:, :, 0, :], bq[:, p, :, :, 1])
                c.link(V.tensor_scalar(q8[:, p], bq[:, p, :, :, 1], float(T), None, ALU.mult))
                c.link(V.tensor_scalar(gt[:, :, :, :], gt[:, :, :, :], 0.0, None, ALU.max))
                V.tensor_tensor(q_split[:, :, 1, :], bq[:, p, :, :, 1], q_split[:, :, 0, :], ALU.subtract
                                ).then_inc(s_q, 1)
                c.link(V.tensor_reduce(gt_sum[:, :, :], gt[:, :, :, :], AX.X, ALU.add))
                c.link(V.tensor_tensor(d_sum[:, p], q8[:, p], gt_sum[:, :, :], ALU.subtract))

            def bias2_chain(r, p, c):
                G = 2 * r + p
                dve.wait_ge(s_mv2, G + 1)
                c.link(V.tensor_reduce(wq[:, :, :], mv2.rearrange("p m l i -> p m i l"), AX.X, ALU.add))
                for m in range(KT):
                    ins = V.tensor_scalar(bias2[:, p, m], wq[:, m], sc2T[:, m:m + 1], b2_t[:, m:m + 1],
                                          ALU.mult, ALU.add)
                ins.then_inc(s_bias2, 1)

            def g_low(a):
                dve.wait_ge(s_ghi, KT * (a.n + 1))
                V.tensor_tensor(g_split[:, a.par, 1, KT - 1], g_f32[:, a.par, KT - 1],
                                g_split[:, a.par, 0, KT - 1], ALU.subtract).then_inc(s_glo, 1)

            def set_hubs(a, c):
                columns = hub_columns(dve, regs, a)
                dve.wait_ge(s_g, KT * (a.n + 1))
                uu = u2[:, 0]
                c.link(V.tensor_tensor(u2[:, 1], g_sum[:, a.par], d_sum[:, a.p, :, a.i], ALU.add))
                c.link(V.scalar_tensor_tensor(u2[:, 0], u2[:, 1], DEG / N, q8[:, a.p, :, a.i],
                                              ALU.mult, ALU.subtract))
                c.link(V.tensor_copy(u_split[:, 0, :, 0], uu))
                c.link(V.tensor_tensor(u_split[:, 1, :, 0], uu, u_split[:, 0, :, 0], ALU.subtract))
                dve.wait_ge(s_glo, KT * (a.n + 1))
                for t, v in enumerate(columns):
                    ins = V.tensor_copy(g_split[:, a.par, :, :, bass.ds(v, 1)], u_split[:, :, :, :])
                ins.then_inc(s_hubset, 1)

            def output(a, tiles=range(KT)):
                for u in range(UN):
                    m, hf = divmod(u, NH)
                    if m not in tiles:
                        continue
                    dve.wait_ge(s_gemm2, UN * a.n + u + 1)
                    if hf == 0:
                        dve.wait_ge(s_xb, KT * a.n + m + 1)
                    xs = x_sb[:, a.slot, m, hf * HALF:(hf + 1) * HALF]
                    V.scalar_tensor_tensor(g_f32[:, a.par, m, hf * HALF:(hf + 1) * HALF], ps2[u % 2][:, :], sc2[:, m:m + 1], xs, ALU.mult, ALU.add
                                           ).then_inc(s_o, 1)

            class Chain:
                def __init__(self, n=0):
                    self.n = n

                def link(self, ins):
                    self.n += 1
                    ins.then_inc(s_chain, 1)
                    dve.wait_ge(s_chain, self.n)

                def restart(self):
                    dve.wait_ge(s_chain, self.n)
                    dve.sem_clear(s_chain)
                    self.n = 0

            c = Chain(ch[0])
            for d in range(LEAD + 1):
                bn(ahead(0, 0, 0, d), c)
                norm(ahead(0, 0, 0, d), c)
                if d == GB - 1:
                    rank_top(0, 0, c)
                    rank_index(0, 0, c)
                    rank_next(0, 0, c)
                    means(0, 0, c)
                    gather(0, 0)
            c.restart()

            def steps(r, p):
                q = nxt(r, p)
                for i in range(GB):
                    last, new = ahead(r, p, i, -1), ahead(r, p, i, LEAD + 1)
                    ranks = i == GB - 1 and q
                    if last and i > 0:
                        set_hubs(last, c)
                    if i == 1:
                        bias2_chain(r, p, c)
                    if new and i > 0:
                        bn(new, c)
                    if last:
                        output(last, (0,))
                    if i == 0:
                        bias1_chain(r, p, c)
                        q_chain(r, p, c)
                        if new:
                            bn(new, c)
                    if ranks:
                        rank_top(*q, c)
                    if last:
                        output(last, (1,))
                    if ranks:
                        rank_index(*q, c)
                    if new:
                        norm(new, c)
                    if i == 0:
                        g_low(At(r, p, 0))
                    if ranks:
                        means(*q, c)
                        rank_next(*q, c)
                        set_hubs(At(r, p, i), c)
                        gather(*q)
                c.restart()

            run_groups(dve, steps)
            a = At(NG // 2 - 1, 1, GB - 1)
            set_hubs(a, c)
            output(a)

        @block.tensor
        def _(pe):
            MM = nc.tensor.matmul
            pe.wait_ge(consts, 3)
            pe.wait_ge(w_split_ready, 1)
            for w in range(2):
                for m in range(KT):
                    for k in range(KT):
                        ins = nc.tensor.transpose(
                            ps1[m][:, w].bitcast(F16)[:, k * P:(k + 1) * P],
                            w_part[:, w, m, k * P:(k + 1) * P], ident[:, :])
            ins.then_inc(w_transposed, 1)
            pe.wait_ge(w_ready, 1)

            def colsum(a):
                pe.wait_ge(s_hlo, KT * (a.n + 1))
                if a.i == 0:
                    ge(pe, s_csread, a.G)
                for k in range(KT):
                    for l in range(2):
                        for hf in range(NH):
                            ins = MM(ps_cs[32 * hf:32 * hf + 32, :], onehot[:, 32 - a.i:64 - a.i],
                                     h_split[:, a.slot, l, k, hf * HALF:(hf + 1) * HALF],
                                     start=(a.i == 0 and k == 0 and l == 0),
                                     stop=(a.i == GB - 1 and k == KT - 1 and l == 1))
                ins.then_inc(s_cs, 1)

            PARTS = [(0, (0, 1)), (1, (0,))]

            def gemm1(a):
                pe.wait_ge(s_hlo, KT * (a.n + 1))
                for m in range(KT):
                    ge(pe, s_g, KT * (a.n - 1) + m + 1)
                    for w, ls in PARTS:
                        for k in range(KT):
                            for l in ls:
                                for hf in range(NH):
                                    ins = MM(ps1[m][:, hf], w_t[:, w, k, m * P:(m + 1) * P],
                                             h_split[:, a.slot, l, k, hf * HALF:(hf + 1) * HALF],
                                             start=(w == 0 and k == 0 and l == 0),
                                             stop=(w == 1 and k == KT - 1))
                    ins.then_inc(s_gemm1, 1)

            def gemm2(a, units):
                pe.wait_ge(s_hubset, a.n + 1)
                for u in units:
                    m, hf = divmod(u, NH)
                    ge(pe, s_o, UN * a.n + u - 1)
                    for w, ls in PARTS:
                        for k in range(KT):
                            for l in ls:
                                ins = MM(ps2[u % 2][:, :], w_t[:, w, k, m * P:(m + 1) * P],
                                         g_split[:, a.par, l, k, hf * HALF:(hf + 1) * HALF],
                                         start=(w == 0 and k == 0 and l == 0),
                                         stop=(w == 1 and k == KT - 1))
                    ins.then_inc(s_gemm2, 1)

            def matvec1(r, p):
                G = 2 * r + p
                pe.wait_ge(s_hubs, 2 * (G + 1))
                ge(pe, s_bias2, G)
                for m in range(KT):
                    for w in range(2):
                        for k in range(KT):
                            ins = MM(mv1[:, m].rearrange("p i l j -> p (i l j)"),
                                     w_t[:, w, k, m * P:(m + 1) * P],
                                     mv_in[:, k].rearrange("p i j -> p (i j)"),
                                     start=(w == 0 and k == 0), stop=(w == 1 and k == KT - 1))
                ins.then_inc(s_mv1, 1)

            def matvec2(r, p):
                G = 2 * r + p
                pe.wait_ge(s_q, G + 1)
                for m in range(KT):
                    for w in range(2):
                        for k in range(KT):
                            ins = MM(mv2[:, m].rearrange("p l i -> p (l i)"),
                                     w_t[:, w, k, m * P:(m + 1) * P],
                                     q_split[:, k].rearrange("p l i -> p (l i)"),
                                     start=(w == 0 and k == 0), stop=(w == 1 and k == KT - 1))
                ins.then_inc(s_mv2, 1)

            for i in range(GB):
                colsum(At(0, 0, i))
            colsum(ahead(0, 0, 0, GB))

            def steps(r, p):
                for i in range(GB):
                    gemm1(At(r, p, i))
                    b = ahead(r, p, i, -1)
                    if b:
                        gemm2(b, range(NH))
                    if i == 0:
                        matvec1(r, p)
                    if b:
                        gemm2(b, range(NH, UN))
                    if b := ahead(r, p, i, LEAD):
                        colsum(b)
                    if i == 0:
                        matvec2(r, p)

            run_groups(pe, steps)
            gemm2(At(NG // 2 - 1, 1, GB - 1), range(UN))


_OUT = ((32, 256, 1024), "float32")


def kernel(x, adj, L0_gnn_b1, L0_gnn_b2):
    import numpy as np
    import concourse.bacc as bacc
    from concourse.bass_utils import run_bass_kernel_spmd

    nc = bacc.Bacc("TRN2", target_bir_lowering=False, num_devices=1)
    arrays, args = {}, []
    for name, a in (("x", x), ("adj", adj), ("b1", L0_gnn_b1), ("b2", L0_gnn_b2)):
        a = np.ascontiguousarray(a)
        arrays[f"in_{name}"] = a
        args.append(nc.dram_tensor(f"in_{name}", a.shape, mybir.dt.from_np(a.dtype), kind="ExternalInput").ap())
    shape, dtype = _OUT
    o = nc.dram_tensor("out_0", shape, mybir.dt.from_np(np.dtype(dtype)), kind="ExternalOutput").ap()
    adjacency_gnn_kernel(nc, *args, o)
    r = run_bass_kernel_spmd(nc, [arrays], core_ids=[0])
    return r.results[0]["out_0"]
```

```python
import concourse.bass as bass
from concourse import mybir
from contextlib import ExitStack


def adjacency_gnn_kernel(nc, x, adj, b1, b2, out):
    F32 = mybir.dt.float32
    F16 = mybir.dt.float16
    U32 = mybir.dt.uint32
    I32 = mybir.dt.int32
    ALU = mybir.AluOpType
    ACT = mybir.ActivationFunctionType
    AX = mybir.AxisListType

    B, S, N = x.shape
    P = 128
    KT = S // P
    HALF = 512
    NH = N // HALF
    GB = 4
    NG = B // GB
    SLOTS = 2 * GB
    T = 8
    C = T + 1
    DEG = float(T + 1)
    HS = 1024.0
    EPS = 1e-5
    TINY = 2.0 ** -60

    ctx = ExitStack()
    with ctx:
        def sb(name, shape, dt=F32):
            return ctx.enter_context(nc.sbuf_tensor(name, shape, dt))

        def sem(name):
            return ctx.enter_context(nc.semaphore(name))

        x_sb = sb("x_sb", [P, SLOTS, KT, N])
        h_split = sb("h_split", [P, SLOTS, 2, KT, N], F16)
        h_f32 = sb("h_f32", [P, 2, KT, N])
        g_f32 = sb("g_f32", [P, 2, KT, N])
        g_split = sb("g_split", [P, 2, 2, KT, N], F16)
        adj_sb = sb("adj_sb", [P, KT, S])
        w_part = sb("w_part", [P, 2, KT, S], F16)
        w_t = sb("w_t", [P, 2, KT, S], F16)
        ident = sb("ident", [P, P], F16)
        onehot = sb("onehot", [P, 2 * 32], F16)
        eps_t = sb("eps_t", [P, 1])
        b1_t = sb("b1_t", [P, KT])
        b2_t = sb("b2_t", [P, KT])
        setup = sb("setup", [P, 24, KT])
        sc1 = sb("sc1", [P, KT, 2])
        b1p = sb("b1p", [P, KT, 2])
        sc2 = sb("sc2", [P, KT])
        sc2T = sb("sc2T", [P, KT])
        stats = sb("stats", [P, 2, KT, NH, 6])
        meanvar = sb("meanvar", [P, 2, KT, 2])
        std = sb("std", [P, 2, KT])
        nrm = sb("nrm", [P, 5, KT])
        rstd = sb("rstd", [P, 2, KT])
        nmr = sb("nmr", [P, 2, KT])
        h_sum = sb("h_sum", [P, SLOTS, KT])
        g_sum = sb("g_sum", [P, 2, KT])
        fv = sb("fv", [GB, N])
        fv_rest = sb("fv_rest", [GB, N])
        top8 = sb("top8", [GB, 8])
        next8 = sb("next8", [GB, 8])
        rank_idx = sb("rank_idx", [GB, 2, 20], U32)
        fv_min = sb("fv_min", [GB, 2])
        zero_flag = sb("zero_flag", [P, 2])
        flag_int = sb("flag_int", [P, 1], I32)
        mv_in = sb("mv_in", [P, KT, GB, 2 * C], F16)
        mv_sum = sb("mv_sum", [P, KT, GB, C])
        hub_sum = sb("hub_sum", [P, KT, GB, 2])
        bq = sb("bq", [P, 2, KT, GB, 2])
        gt = sb("gt", [P, KT, GB, T])
        gt_sum = sb("gt_sum", [P, KT, GB])
        d_sum = sb("d_sum", [P, 2, KT, GB])
        q8 = sb("q8", [P, 2, KT, GB])
        q_split = sb("q_split", [P, KT, 2, GB], F16)
        wq = sb("wq", [P, KT, GB])
        bias2 = sb("bias2", [P, 2, KT, GB])
        u2 = sb("u2", [P, 2, KT])
        u_split = sb("u_split", [P, 2, KT, 1], F16)

        ps1 = [ctx.enter_context(nc.psum_tensor(f"ps1_{m}", [P, NH, HALF], F32)) for m in range(KT)]
        ps2 = [ctx.enter_context(nc.psum_tensor(f"ps2_{u}", [P, HALF], F32)) for u in range(2)]
        ps_cs = ctx.enter_context(nc.psum_tensor("ps_cs", [P, HALF], F32))
        ps_mv = ctx.enter_context(nc.psum_tensor("ps_mv", [P, HALF], F32))
        mv1 = ps_mv[:, 0:KT * GB * 2 * C].rearrange("p (m i l j) -> p m i l j", m=KT, i=GB, l=2)
        mv2 = ps_mv[:, 256:256 + KT * 2 * GB].rearrange("p (m l i) -> p m l i", m=KT, l=2)

        consts = sem("consts")
        in_small = sem("in_small")
        setup_dve = sem("setup_dve")
        setup_pool = sem("setup_pool")
        w_split_ready = sem("w_split_ready")
        w_transposed = sem("w_transposed")
        w_ready = sem("w_ready")
        x_in = [[sem(f"x_in{s}_{k}") for k in range(KT)] for s in range(SLOTS)]
        stored = [[sem(f"stored{s}_{k}") for k in range(KT)] for s in range(2)]
        s_chain = sem("dve_chain")
        s_var = sem("var_ready")
        s_std = sem("std_ready")
        s_norm = sem("norm_ready")
        s_h = sem("h_ready")
        s_hhi = sem("h_hi_ready")
        s_hlo = sem("h_lo_ready")
        s_cs = sem("colsum_done")
        s_csread = sem("colsum_read")
        s_rank = sem("hubs_ranked")
        s_hubs = sem("hubs_gathered")
        s_mv1 = sem("matvec1_done")
        s_q = sem("q_ready")
        s_bias1 = sem("bias1_ready")
        s_mv2 = sem("matvec2_done")
        s_bias2 = sem("bias2_ready")
        s_gemm1 = sem("gemm1_done")
        s_g = sem("g_ready")
        s_ghi = sem("g_hi_ready")
        s_glo = sem("g_lo_ready")
        s_hubset = sem("hub_columns_set")
        s_gemm2 = sem("gemm2_done")
        s_xb = sem("x_with_bias2")
        s_o = sem("out_ready")

        s_flag = sem("flag_ready")
        s_flagrows = sem("flag_rows_ready")
        a_x = sem("any_x_in")
        a_var = sem("any_var_ready")
        a_std = sem("any_std_ready")
        a_const = sem("any_const_ready")
        a_h = sem("any_h_ready")
        a_rows = sem("any_rows_ready")
        a_pe = sem("any_psum_filled")
        a_dve = sem("any_psum_read")
        a_stored = sem("any_stored")

        UN = KT * NH

        NT = N // P
        any_x, any_h, any_g = x_sb[:, 0], x_sb[:, 1], x_sb[:, 2]
        any_y = x_sb[:, 3].rearrange("p k n -> p (k n)").rearrange("p (j s) -> p j s", j=NT)
        any_adj = x_sb[:, 4:8].rearrange("p a k n -> p (a k) n")
        any_out = h_f32[:, 0]
        any_rdeg = h_f32[:, 1, 0]
        any_ones = h_f32[:, 1, 1, 0:P]
        any_w = adj_sb
        any_sum = g_f32[0:1, 0, 0]
        any_sum1, any_sum2 = g_f32[0:1, 0, 1], g_f32[0:1, 1, 0]
        row_some, row_zero, row_hub, row_tie = (g_split[0:1, 0, l, k] for l in range(2) for k in range(KT))
        COUNTS = (NH, NT, NT * NH, NH, UN, NT, UN)
        IT_SUM, IT_Y1, IT_ADJ, IT_DEG, IT_G, IT_Y2, IT_OUT = (sum(COUNTS[:z]) for z in range(7))
        ITEMS = sum(COUNTS)
        BANKS = KT * NH

        def any_bank(e):
            return ps1[e % BANKS // NH][:, e % NH, :]

        def when_flagged(eng, body):
            eng.wait_ge(s_flag, 1)
            flag = eng.alloc_register("flag_" + body.__name__)
            eng.load([flag], flag_int[0:1, 0:1])
            with eng.If_ne(flag, 0):
                with eng.Fori(0, B) as n:
                    body(n)

        def ge(eng, s, v):
            if not isinstance(v, int) or v > 0:
                eng.wait_ge(s, v)

        class At:
            def __init__(self, r, p, i):
                self.i, self.p = i, p
                self.n = 2 * GB * r + GB * p + i
                self.G = 2 * r + p
                self.r = r
                self.slot = GB * p + i
                self.par = i % 2

        def ahead(r, p, i, d):
            t = GB * p + i + d
            a = At(r + t // SLOTS, t % SLOTS // GB, t % GB)
            return a if not isinstance(a.n, int) or 0 <= a.n < B else None

        def run_groups(eng, steps):
            steps(0, 0)
            with eng.Fori(0, NG // 2 - 2) as r:
                steps(r, 1)
                steps(r + 1, 0)
            for r, p in ((NG // 2 - 2, 1), (NG // 2 - 1, 0), (NG // 2 - 1, 1)):
                steps(r, p)

        def nxt(r, p):
            q = (r, 1) if p == 0 else (r + 1, 0)
            return None if isinstance(r, int) and q[0] == NG // 2 else q

        LEAD = 5

        def hub_columns(eng, regs, a):
            eng.load(regs, rank_idx[a.i:a.i + 1, a.p, 4:4 + T])
            return [eng.snap(g, min_val=0, max_val=N - 1) for g in regs]

        def gather_hubs(eng, ops, regs, a):
            for t, v in enumerate(hub_columns(eng, regs, a)):
                ins = ops.tensor_copy(
                    mv_in[:, :, a.i, :].rearrange("p k (l j) -> p l k j", l=2)[:, :, :, t:t + 1],
                    h_split[:, a.slot, :, :, bass.ds(v, 1)])
            return ins

        DVE_GATHERS = 1

        block = ctx.enter_context(nc.Block())

        @block.sync
        def _(sp):
            def load(slot, n, k):
                sp.dma_start(x_sb[:, slot, k], x[bass.ds(n, 1), k * P:(k + 1) * P, :].rearrange("a p n -> p (a n)")
                             ).then_inc(x_in[slot][k], 16)

            for k in range(KT):
                load(0, 0, k)
            sp.dma_start(adj_sb[:, :, :], adj.rearrange("(m p) s -> p m s", p=P)).then_inc(in_small, 16)
            sp.dma_start(b1_t[:, :], b1.rearrange("(m p) -> p m", p=P),
                         allow_slow_non_contiguous=True).then_inc(in_small, 16)
            sp.dma_start(b2_t[:, :], b2.rearrange("(m p) -> p m", p=P),
                         allow_slow_non_contiguous=True).then_inc(in_small, 16)
            for s in range(1, SLOTS):
                for k in range(KT):
                    load(s, s, k)

            def store(a, reload):
                for m in range(KT):
                    sp.wait_ge(s_o, UN * a.n + NH * (m + 1))
                    dst = out[bass.ds(a.n, 1), m * P:(m + 1) * P, :].rearrange("a p n -> p (a n)")
                    sp.dma_start(dst, g_f32[:, a.par, m]).then_inc(stored[a.par][m], 16)
                    if reload:
                        load(a.slot, a.n + SLOTS, m)

            def steps(r, p):
                for i in range(GB):
                    a = ahead(r, p, i, -1)
                    if a:
                        store(a, not isinstance(a.n, int) or a.n + SLOTS < B)

            run_groups(sp, steps)
            store(At(NG // 2 - 1, 1, GB - 1), False)
            for s in range(2):
                for m in range(KT):
                    sp.wait_ge(stored[s][m], 16 * (B // 2))

            def any_sp(n):
                for k in range(KT):
                    sp.dma_start(any_x[:, k], x[bass.ds(n, 1), k * P:(k + 1) * P, :].rearrange("a p n -> p (a n)")
                                 ).then_inc(a_x, 16)
                sp.wait_ge(a_dve, ITEMS * n + ITEMS)
                for k in range(KT):
                    sp.dma_start(out[bass.ds(n, 1), k * P:(k + 1) * P, :].rearrange("a p n -> p (a n)"),
                                 any_out[:, k]).then_inc(a_stored, 16)
                sp.wait_ge(a_stored, 16 * KT)
                sp.sem_clear(a_stored)

            when_flagged(sp, any_sp)

        @block.gpsimd
        def _(pool):
            pool.memset(ident[:, :], 0.0).then_inc(setup_pool, 1)
            pool.memset(onehot[:, :], 0.0).then_inc(setup_pool, 1)
            pool.memset(eps_t[:, :], EPS).then_inc(consts, 1)
            pool.wait_ge(setup_pool, 2)
            pool.affine_select(out=ident[:, :], in_=ident[:, :], compare_op=ALU.not_equal, fill=1.0,
                               base=0, pattern=[[-1, P]], channel_multiplier=1).then_inc(consts, 1)
            pool.memset(onehot[:, 32:33], 1.0).then_inc(consts, 1)

            def h_low(a):
                for k in range(KT):
                    pool.wait_ge(s_hhi, KT * a.n + k + 1)
                    pool.tensor_tensor(h_split[:, a.slot, 1, k], h_f32[:, a.par, k],
                                       h_split[:, a.slot, 0, k], ALU.subtract).then_inc(s_hlo, 1)

            def g_low(a):
                for m in range(KT if a.i else KT - 1):
                    pool.wait_ge(s_ghi, KT * a.n + m + 1)
                    pool.tensor_tensor(g_split[:, a.par, 1, m], g_f32[:, a.par, m],
                                       g_split[:, a.par, 0, m], ALU.subtract).then_inc(s_glo, 1)

            for d in range(LEAD):
                h_low(ahead(0, 0, 0, d))
                if d == 0:
                    pool.wait_ge(setup_dve, 1)
                    pool.partition_all_reduce(setup[:, 11, 0:1], setup[:, 10, 0:1], P,
                                              bass.bass_isa.ReduceOp.max).then_inc(setup_pool, 1)

            regs = [pool.alloc_register(f"pool_hub{t}") for t in range(T)]

            def gather(r, p, count):
                pool.wait_ge(consts, 3)
                pool.wait_ge(s_rank, count)
                for i in range(DVE_GATHERS, GB):
                    ins = gather_hubs(pool, pool, regs, At(r, p, i))
                ins.then_inc(s_hubs, 1)

            gather(0, 0, 1)

            def steps(r, p):
                for i in range(GB):
                    q = nxt(r, p) if i == GB - 1 else None
                    if q:
                        count = 2 * q[0] + q[1] + 1
                        count = count if isinstance(count, int) else pool.snap(count)
                        pool.wait_ge(s_csread, count)
                    if b := ahead(r, p, i, LEAD):
                        h_low(b)
                    g_low(At(r, p, i))
                    if q:
                        gather(*q, count)

            run_groups(pool, steps)
            pool.wait_ge(s_flagrows, 1)
            pool.partition_all_reduce(zero_flag[:, 1:2], zero_flag[:, 0:1], P, bass.bass_isa.ReduceOp.max
                                      ).then_inc(setup_pool, 1)
            pool.wait_ge(setup_pool, 4)
            pool.tensor_copy(flag_int[:, :], zero_flag[:, 1:2]).then_inc(s_flag, 1)

        @block.scalar
        def _(act):
            act.wait_ge(consts, 3)

            def std_dev(a):
                act.wait_ge(s_var, a.n + 1)
                nc.scalar.activation(std[:, a.par], meanvar[:, a.par, :, 1], ACT.Sqrt, bias=eps_t[:, 0:1]
                                     ).then_inc(s_std, 1)

            def h_tiles(a):
                act.wait_ge(s_norm, a.n + 1)
                for k in range(KT):
                    ge(act, s_hlo, KT * (a.n - 2) + k + 1)
                    nc.scalar.activation(h_f32[:, a.par, k], x_sb[:, a.slot, k], ACT.Relu,
                                         bias=nmr[:, a.par, k:k + 1], scale=rstd[:, a.par, k:k + 1],
                                         accum_out=h_sum[:, a.slot, k:k + 1]).then_inc(s_h, 1)
                for k in range(KT):
                    act.wait_ge(s_h, KT * a.n + k + 1)
                    nc.scalar.activation(h_split[:, a.slot, 0, k], h_f32[:, a.par, k], ACT.Copy
                                         ).then_inc(s_hhi, 1)

            def add_bias2(a):
                act.wait_ge(s_bias2, a.G + 1)
                for m in range(KT):
                    nc.scalar.activation(x_sb[:, a.slot, m], x_sb[:, a.slot, m], ACT.Identity,
                                         bias=bias2[:, a.p, m, a.i:a.i + 1]).then_inc(s_xb, 1)

            def g_tiles(a):
                act.wait_ge(s_bias1, a.G + 1)
                for m in range(KT):
                    act.wait_ge(s_gemm1, KT * a.n + m + 1)
                    ge(act, stored[a.par][m], 16 * (a.n // 2 if isinstance(a.n, int) else
                                                    GB * a.r + (GB * a.p + a.i) // 2))
                    if m == 0:
                        ge(act, s_hubset, a.n - 1)
                    nc.scalar.activation(g_f32[:, a.par, m], ps1[m][:, :, :].rearrange("p a n -> p (a n)"),
                                         ACT.Relu, bias=bq[:, a.p, m, a.i, 0:1], scale=sc1[:, m, 0:1],
                                         accum_out=g_sum[:, a.par, m:m + 1]).then_inc(s_g, 1)
                ge(act, s_gemm2, UN * (a.n - 1))
                for m in range(KT):
                    act.wait_ge(s_g, KT * a.n + m + 1)
                    nc.scalar.activation(g_split[:, a.par, 0, m], g_f32[:, a.par, m], ACT.Copy
                                         ).then_inc(s_ghi, 1)

            std_dev(At(0, 0, 0))
            for d in range(LEAD):
                std_dev(ahead(0, 0, 0, d + 1))
                h_tiles(ahead(0, 0, 0, d))

            def steps(r, p):
                for i in range(GB):
                    if b := ahead(r, p, i, LEAD):
                        h_tiles(b)
                    if b := ahead(r, p, i, -1):
                        add_bias2(b)
                    g_tiles(At(r, p, i))
                    if b := ahead(r, p, i, LEAD + 1):
                        std_dev(b)

            run_groups(act, steps)
            add_bias2(At(NG // 2 - 1, 1, GB - 1))

            def any_act(n):
                act.wait_ge(a_var, n + 1)
                nc.scalar.activation(std[:, 0], meanvar[:, 0, :, 1], ACT.Sqrt, bias=eps_t[:, 0:1]
                                     ).then_inc(a_std, 1)

            when_flagged(act, any_act)

        @block.vector
        def _(dve):
            V = nc.vector

            class Chain:
                def __init__(self, n=0):
                    self.n = n

                def link(self, ins):
                    self.n += 1
                    ins.then_inc(s_chain, 1)
                    dve.wait_ge(s_chain, self.n)

                def restart(self):
                    dve.wait_ge(s_chain, self.n)
                    dve.sem_clear(s_chain)
                    self.n = 0

            ROWMAX, ROWSUM, CPOW, CINV, BND, BPOW, PINV, PSC = range(8)

            def st(j):
                return setup[:, j, :]

            def split_weights(link):
                dve.wait_ge(in_small, 48)
                link(V.tensor_reduce(st(ROWMAX), adj_sb[:, :, :], AX.X, ALU.max, apply_absolute_value=True))
                link(V.tensor_reduce(st(ROWSUM), adj_sb[:, :, :], AX.X, ALU.add, apply_absolute_value=True))
                link(V.tensor_scalar(st(ROWMAX), st(ROWMAX), TINY, None, ALU.max))
                link(V.tensor_scalar(st(CPOW).bitcast(I32), st(ROWMAX).bitcast(I32), 0x7F800000, None,
                                     ALU.bitwise_and))
                link(V.reciprocal(st(CINV), st(CPOW)))
                link(V.tensor_scalar(st(CINV), st(CINV), 2.0 ** 13, None, ALU.mult))
                for m in range(KT):
                    link(V.tensor_scalar(adj_sb[:, m], adj_sb[:, m], setup[:, CINV, m:m + 1], None, ALU.mult))
                link(V.tensor_copy(w_part[:, 0], adj_sb[:, :, :]))
                link(V.tensor_tensor(w_part[:, 1], adj_sb[:, :, :], w_part[:, 0], ALU.subtract))
                V.tensor_scalar(st(BND), b1_t[:, :], 0.0, None, ALU.add).then_inc(w_split_ready, 1)
                dve.wait_ge(w_split_ready, 1)
                link(V.tensor_reduce(setup[:, BND, :].rearrange("p (m o) -> p m o", o=1),
                                     b1_t[:, :].rearrange("p (m o) -> p m o", o=1), AX.X, ALU.max,
                                     apply_absolute_value=True))
                link(V.scalar_tensor_tensor(st(BND), st(ROWSUM), 32.0, st(BND), ALU.mult, ALU.add))
                link(V.tensor_reduce(setup[:, 10, 0:1], st(BND), AX.X, ALU.max))
                link(V.tensor_scalar(setup[:, 10, 0:1], setup[:, 10, 0:1], TINY, None, ALU.max))
                V.tensor_copy(setup[:, 12, 0:1], setup[:, 10, 0:1]).then_inc(setup_dve, 1)

            def scales(link):
                dve.wait_ge(setup_pool, 3)
                link(V.tensor_scalar(setup[:, BPOW, 0:1].bitcast(I32), setup[:, 11, 0:1].bitcast(I32),
                                     0x7F800000, None, ALU.bitwise_and))
                link(V.reciprocal(setup[:, PSC, 0:1], setup[:, BPOW, 0:1]))
                link(V.tensor_scalar(setup[:, PSC, 0:1], setup[:, PSC, 0:1], 2.0 ** 11, None, ALU.mult))
                link(V.tensor_scalar(setup[:, PINV, 0:1], setup[:, BPOW, 0:1], 2.0 ** -11, None, ALU.mult))
                psc, pinv = setup[:, PSC, 0:1], setup[:, PINV, 0:1]
                link(V.tensor_scalar(sc1[:, :, 1], st(CPOW), 2.0 ** -13 / HS, psc, ALU.mult, ALU.mult))
                link(V.tensor_scalar(sc1[:, :, 0], sc1[:, :, 1], 1.0 / DEG, None, ALU.mult))
                link(V.tensor_scalar(sc2[:, :], st(CPOW), 2.0 ** -13 / DEG, pinv, ALU.mult, ALU.mult))
                link(V.tensor_scalar(sc2T[:, :], sc2[:, :], float(T), None, ALU.mult))
                for c in range(2):
                    link(V.tensor_scalar(b1p[:, :, c], b1_t[:, :], psc, None, ALU.mult))
                dve.wait_ge(w_transposed, 1)
                for w in range(2):
                    for m in range(KT):
                        ins = V.tensor_copy(w_t[:, w, :, m * P:(m + 1) * P],
                                            ps1[m][:, w].bitcast(F16)[:, 0:KT * P].rearrange("p (k o) -> p k o", k=KT))
                ins.then_inc(w_ready, 1)

            def bn(a, c):
                for k in range(KT):
                    dve.wait_ge(x_in[a.slot][k], 16 * (a.r + 1))
                    for hf in range(NH):
                        ins = V.bn_stats(stats[:, a.par, k, hf], x_sb[:, a.slot, k, hf * HALF:(hf + 1) * HALF])
                c.link(ins)
                for k in range(KT):
                    ins = V.bn_aggr(meanvar[:, a.par, k], stats[:, a.par, k].rearrange("p h s -> p (h s)"))
                ins.then_inc(s_var, 1)

            def norm(a, c):
                mean, var = meanvar[:, a.par, :, 0], meanvar[:, a.par, :, 1]
                y0, ve, ysq, t1, t2 = (nrm[:, z] for z in range(5))
                dve.wait_ge(s_std, a.n + 1)
                V.reciprocal(y0, std[:, a.par])
                c.link(V.tensor_scalar(ve, var, EPS, None, ALU.add))
                c.link(V.tensor_tensor(ysq, y0, y0, ALU.mult))
                c.link(V.tensor_tensor(t1, ysq, ve, ALU.mult))
                c.link(V.tensor_scalar(t2, t1, -0.5, 1.5, ALU.mult, ALU.add))
                c.link(V.scalar_tensor_tensor(rstd[:, a.par], y0, HS, t2, ALU.mult, ALU.mult))
                V.scalar_tensor_tensor(nmr[:, a.par], mean, -1.0, rstd[:, a.par], ALU.mult, ALU.mult
                                       ).then_inc(s_norm, 1)

            def rank_top(r, p, c):
                G = 2 * r + p
                dve.wait_ge(s_cs, GB * (G + 1))
                for hf in range(NH):
                    ins = V.tensor_scalar(fv[:, hf * HALF:(hf + 1) * HALF], ps_cs[32 * hf:32 * hf + GB, :],
                                          0.0, None, ALU.add)
                ins.then_inc(s_csread, 1)
                dve.wait_ge(consts, 3)
                dve.wait_ge(s_csread, G + 1)
                idx = rank_idx[:, p]
                c.link(V.max(top8[:, :], fv[:, :]))

            def rank_index(r, p, c):
                idx = rank_idx[:, p]
                V.max_index(idx[:, 3:11], top8[:, :], fv[:, :])
                c.link(V.match_replace(fv_rest[:, :], top8[:, :], fv[:, :], -1.0))

            def rank_next(r, p, c):
                idx = rank_idx[:, p]
                c.link(V.max(next8[:, :], fv_rest[:, :]))
                V.max_index(idx[:, 11:19], next8[:, :], fv_rest[:, :]).then_inc(s_rank, 1)

            def smallest_sum(c):
                c.link(V.tensor_reduce(fv_min[:, 1:2], fv[:, :], AX.X, ALU.min))
                c.link(V.tensor_tensor(fv_min[:, 0:1], fv_min[:, 0:1], fv_min[:, 1:2], ALU.min))

            regs = [dve.alloc_register(f"hub{t}") for t in range(T)]

            def gather(r, p):
                count = 2 * r + p + 1
                count = count if isinstance(count, int) else dve.snap(count)
                dve.wait_ge(consts, 3)
                dve.wait_ge(s_rank, count)
                for i in range(DVE_GATHERS):
                    ins = gather_hubs(dve, V, regs, At(r, p, i))
                ins.then_inc(s_hubs, 1)

            def means(r, p, c):
                G = 2 * r + p
                dve.wait_ge(s_hlo, KT * (At(r, p, 0).n + GB))
                ge(dve, s_mv1, G)
                sums = h_sum[:, GB * p:GB * (p + 1), :].rearrange("p i k -> p k i")
                c.link(V.tensor_scalar(mv_in[:, :, :, T], sums, 1.0 / N, None, ALU.mult))
                c.link(V.scalar_tensor_tensor(mv_in[:, :, :, C + T], sums, 1.0 / N, mv_in[:, :, :, T],
                                              ALU.mult, ALU.subtract))

            def bias1_chain(r, p, c):
                G = 2 * r + p
                dve.wait_ge(s_mv1, G + 1)
                for m in range(KT):
                    ins = V.tensor_reduce(mv_sum[:, m], mv1[:, m].rearrange("p i l j -> p i j l"), AX.X, ALU.add)
                c.link(ins)
                V.tensor_copy(hub_sum[:, :, :, 1], mv_sum[:, :, :, T])
                c.link(V.tensor_reduce(hub_sum[:, :, :, 0], mv_sum[:, :, :, 0:T], AX.X, ALU.add))
                for m in range(KT):
                    ins = V.tensor_tensor(hub_sum[:, m], hub_sum[:, m],
                                          sc1[:, m:m + 1, :].to_broadcast([P, GB, 2]), ALU.mult)
                c.link(ins)
                for m in range(KT):
                    ins = V.tensor_tensor(bq[:, p, m], hub_sum[:, m],
                                          b1p[:, m:m + 1, :].to_broadcast([P, GB, 2]), ALU.add)
                ins.then_inc(s_bias1, 1)

            def q_chain(r, p, c):
                G = 2 * r + p
                dve.wait_ge(s_bias1, G + 1)
                c.link(V.tensor_scalar(bq[:, p, :, :, 1], bq[:, p, :, :, 1], 0.0, None, ALU.max))
                for m in range(KT):
                    ins = V.tensor_scalar(gt[:, m], mv_sum[:, m, :, 0:T], sc1[:, m, 0:1], None, ALU.mult)
                c.link(ins)
                for m in range(KT):
                    V.tensor_tensor(gt[:, m], gt[:, m], bq[:, p, m, :, 0:1].to_broadcast([P, GB, T]), ALU.add)
                V.tensor_copy(q_split[:, :, 0, :], bq[:, p, :, :, 1])
                c.link(V.tensor_scalar(q8[:, p], bq[:, p, :, :, 1], float(T), None, ALU.mult))
                c.link(V.tensor_scalar(gt[:, :, :, :], gt[:, :, :, :], 0.0, None, ALU.max))
                V.tensor_tensor(q_split[:, :, 1, :], bq[:, p, :, :, 1], q_split[:, :, 0, :], ALU.subtract
                                ).then_inc(s_q, 1)
                c.link(V.tensor_reduce(gt_sum[:, :, :], gt[:, :, :, :], AX.X, ALU.add))
                c.link(V.tensor_tensor(d_sum[:, p], q8[:, p], gt_sum[:, :, :], ALU.subtract))

            def bias2_chain(r, p, c):
                G = 2 * r + p
                dve.wait_ge(s_mv2, G + 1)
                c.link(V.tensor_reduce(wq[:, :, :], mv2.rearrange("p m l i -> p m i l"), AX.X, ALU.add))
                for m in range(KT):
                    ins = V.tensor_scalar(bias2[:, p, m], wq[:, m], sc2T[:, m:m + 1], b2_t[:, m:m + 1],
                                          ALU.mult, ALU.add)
                ins.then_inc(s_bias2, 1)

            def g_low(a):
                dve.wait_ge(s_ghi, KT * (a.n + 1))
                V.tensor_tensor(g_split[:, a.par, 1, KT - 1], g_f32[:, a.par, KT - 1],
                                g_split[:, a.par, 0, KT - 1], ALU.subtract).then_inc(s_glo, 1)

            def set_hubs(a, c):
                columns = hub_columns(dve, regs, a)
                dve.wait_ge(s_g, KT * (a.n + 1))
                uu = u2[:, 0]
                c.link(V.tensor_tensor(u2[:, 1], g_sum[:, a.par], d_sum[:, a.p, :, a.i], ALU.add))
                c.link(V.scalar_tensor_tensor(u2[:, 0], u2[:, 1], DEG / N, q8[:, a.p, :, a.i],
                                              ALU.mult, ALU.subtract))
                c.link(V.tensor_copy(u_split[:, 0, :, 0], uu))
                c.link(V.tensor_tensor(u_split[:, 1, :, 0], uu, u_split[:, 0, :, 0], ALU.subtract))
                dve.wait_ge(s_glo, KT * (a.n + 1))
                for t, v in enumerate(columns):
                    ins = V.tensor_copy(g_split[:, a.par, :, :, bass.ds(v, 1)], u_split[:, :, :, :])
                ins.then_inc(s_hubset, 1)

            def output(a, tiles=range(KT)):
                for u in range(UN):
                    m, hf = divmod(u, NH)
                    if m not in tiles:
                        continue
                    dve.wait_ge(s_gemm2, UN * a.n + u + 1)
                    if hf == 0:
                        dve.wait_ge(s_xb, KT * a.n + m + 1)
                    xs = x_sb[:, a.slot, m, hf * HALF:(hf + 1) * HALF]
                    V.scalar_tensor_tensor(g_f32[:, a.par, m, hf * HALF:(hf + 1) * HALF], ps2[u % 2][:, :], sc2[:, m:m + 1], xs, ALU.mult, ALU.add
                                           ).then_inc(s_o, 1)

            c = Chain()
            V.memset(fv_min[:, :], 1.0)
            V.memset(zero_flag[:, :], 0.0)
            first = [ahead(0, 0, 0, d) for d in range(LEAD + 1)]
            bn(first[0], c)
            bn(first[1], c)
            norm(first[0], c)
            norm(first[1], c)
            bn(first[2], c)
            split_weights(c.link)
            norm(first[2], c)
            bn(first[3], c)
            norm(first[3], c)
            scales(c.link)
            bn(first[4], c)
            norm(first[4], c)
            bn(first[5], c)
            rank_top(0, 0, c)
            rank_index(0, 0, c)
            rank_next(0, 0, c)
            means(0, 0, c)
            gather(0, 0)
            norm(first[5], c)
            c.restart()

            def steps(r, p):
                q = nxt(r, p)
                for i in range(GB):
                    last, new = ahead(r, p, i, -1), ahead(r, p, i, LEAD + 1)
                    ranks = i == GB - 1 and q
                    if last and i > 0:
                        set_hubs(last, c)
                    if i == 1:
                        bias2_chain(r, p, c)
                    if new and i > 0:
                        bn(new, c)
                    if last:
                        output(last, (0,))
                    if i == 0:
                        bias1_chain(r, p, c)
                        q_chain(r, p, c)
                        if new:
                            bn(new, c)
                    if ranks:
                        rank_top(*q, c)
                    if last:
                        output(last, (1,))
                    if ranks:
                        rank_index(*q, c)
                    if new:
                        norm(new, c)
                    if i == 0:
                        g_low(At(r, p, 0))
                    if i == 1:
                        smallest_sum(c)
                        if not q:
                            V.tensor_scalar(zero_flag[0:GB, 0:1], fv_min[:, 0:1], 0.0, None, ALU.is_le
                                            ).then_inc(s_flagrows, 1)
                    if ranks:
                        means(*q, c)
                        rank_next(*q, c)
                        set_hubs(At(r, p, i), c)
                        gather(*q)
                c.restart()

            run_groups(dve, steps)
            a = At(NG // 2 - 1, 1, GB - 1)
            set_hubs(a, c)
            output(a)
            c.restart()

            def any_dve(n):
                c = Chain()
                dve.wait_ge(a_x, 16 * KT * n + 16 * KT)
                c.link(V.memset(any_ones, 1.0))
                c.link(V.tensor_copy(any_w[:, :, :], w_t[:, 0]))
                c.link(V.tensor_tensor(any_w[:, :, :], any_w[:, :, :], w_t[:, 1], ALU.add))
                c.link(V.tensor_scalar(setup[:, CINV], setup[:, CPOW], 2.0 ** -13, None, ALU.mult))
                for k in range(KT):
                    for hf in range(NH):
                        c.link(V.bn_stats(stats[:, 0, k, hf], any_x[:, k, hf * HALF:(hf + 1) * HALF]))
                    c.link(V.bn_aggr(meanvar[:, 0, k], stats[:, 0, k].rearrange("p h s -> p (h s)")))
                V.tensor_scalar(nrm[:, 1], meanvar[:, 0, :, 1], EPS, None, ALU.add).then_inc(a_var, 1)
                dve.wait_ge(a_var, n + 1)
                dve.wait_ge(a_std, n + 1)
                y0, ve, ysq, t1, t2 = (nrm[:, z] for z in range(5))
                c.link(V.reciprocal(y0, std[:, 0]))
                c.link(V.tensor_tensor(ysq, y0, y0, ALU.mult))
                c.link(V.tensor_tensor(t1, ysq, ve, ALU.mult))
                c.link(V.tensor_scalar(t2, t1, -0.5, 1.5, ALU.mult, ALU.add))
                c.link(V.tensor_tensor(rstd[:, 0], y0, t2, ALU.mult))
                c.link(V.scalar_tensor_tensor(nmr[:, 0], meanvar[:, 0, :, 0], -1.0, rstd[:, 0], ALU.mult, ALU.mult))
                for k in range(KT):
                    c.link(V.tensor_scalar(any_h[:, k], any_x[:, k], rstd[:, 0, k:k + 1], nmr[:, 0, k:k + 1],
                                           ALU.mult, ALU.add))
                c.link(V.tensor_scalar(any_h[:, 0], any_h[:, 0], 0.0, None, ALU.max))
                V.tensor_scalar(any_h[:, 1], any_h[:, 1], 0.0, None, ALU.max).then_inc(a_h, 1)

                def filled(e):
                    dve.wait_ge(a_pe, ITEMS * n + (e + 1))

                def read(ins):
                    ins.then_inc(a_dve, 1)

                def half(t, hf):
                    return t[:, hf * HALF:(hf + 1) * HALF]

                sums_read = dve.snap(ITEMS * n + NH)
                for hf in range(NH):
                    filled(IT_SUM + hf)
                    read(V.tensor_scalar(half(any_sum, hf), any_bank(IT_SUM + hf)[0:1, :], 0.0, None, ALU.add))
                dve.wait_ge(consts, 3)
                dve.wait_ge(a_dve, sums_read)
                c.link(V.max(next8[0:1, :], any_sum))
                c.link(V.memset(top8[0:1, :], -2.0))
                c.link(V.tensor_copy(top8[0:1, 0:1], next8[0:1, 0:1]))
                c.link(V.match_replace(any_sum1, top8[0:1, :], any_sum, -1.0))
                c.link(V.max(next8[0:1, :], any_sum1))
                c.link(V.match_replace(any_sum2, next8[0:1, :], any_sum1, -1.0))
                c.link(V.tensor_tensor(row_hub, any_sum1, any_sum2, ALU.not_equal))
                c.link(V.tensor_scalar(row_zero, any_sum, 0.0, None, ALU.is_equal))
                c.link(V.tensor_scalar(row_some, row_zero, -1.0, 1.0, ALU.mult, ALU.add))
                c.link(V.memset(row_tie, 0.0))
                V.memset(row_tie[:, 1:1 + T], 1.0).then_inc(a_rows, 1)

                for j in range(NT):
                    filled(IT_Y1 + j)
                    read(V.tensor_copy(any_y[:, j], any_bank(IT_Y1 + j)[:, 0:S]))
                for j in range(NT):
                    for hf in range(NH):
                        e = IT_ADJ + NH * j + hf
                        filled(e)
                        dst = half(any_adj[:, j], hf)
                        if j * P // HALF != hf:
                            read(V.tensor_scalar(dst, any_bank(e), 1.0, None, ALU.min))
                        else:
                            c.link(V.tensor_scalar(dst, any_bank(e), 1.0, None, ALU.min))
                            diag = any_adj[:, j, j * P:(j + 1) * P]
                            read(V.tensor_tensor(diag, diag, ident[:, :], ALU.max))
                for hf in range(NH):
                    filled(IT_DEG + hf)
                    read(V.reciprocal(half(any_rdeg, hf), any_bank(IT_DEG + hf)))
                dve.wait_ge(a_dve, ITEMS * n + (IT_DEG + NH))
                for u in range(UN):
                    m, hf = divmod(u, NH)
                    filled(IT_G + u)
                    dst = half(any_g[:, m], hf)
                    c.link(V.tensor_tensor(dst, any_bank(IT_G + u), half(any_rdeg, hf), ALU.mult))
                    c.link(V.tensor_scalar(dst, dst, setup[:, CINV, m:m + 1], b1_t[:, m:m + 1], ALU.mult, ALU.add))
                    read(V.tensor_scalar(dst, dst, 0.0, None, ALU.max))
                for j in range(NT):
                    filled(IT_Y2 + j)
                    read(V.tensor_copy(any_y[:, j], any_bank(IT_Y2 + j)[:, 0:S]))
                for u in range(UN):
                    m, hf = divmod(u, NH)
                    filled(IT_OUT + u)
                    dst = half(any_out[:, m], hf)
                    c.link(V.tensor_tensor(dst, any_bank(IT_OUT + u), half(any_rdeg, hf), ALU.mult))
                    c.link(V.tensor_scalar(dst, dst, setup[:, CINV, m:m + 1], b2_t[:, m:m + 1], ALU.mult, ALU.add))
                    read(V.tensor_tensor(dst, dst, half(any_x[:, m], hf), ALU.add))
                c.restart()

            when_flagged(dve, any_dve)

        @block.tensor
        def _(pe):
            MM = nc.tensor.matmul
            pe.wait_ge(consts, 3)
            pe.wait_ge(w_split_ready, 1)
            for w in range(2):
                for m in range(KT):
                    for k in range(KT):
                        ins = nc.tensor.transpose(
                            ps1[m][:, w].bitcast(F16)[:, k * P:(k + 1) * P],
                            w_part[:, w, m, k * P:(k + 1) * P], ident[:, :])
            ins.then_inc(w_transposed, 1)

            def colsum(a):
                pe.wait_ge(s_hlo, KT * (a.n + 1))
                if a.i == 0:
                    ge(pe, s_csread, a.G)
                for k in range(KT):
                    for l in range(2):
                        for hf in range(NH):
                            ins = MM(ps_cs[32 * hf:32 * hf + 32, :], onehot[:, 32 - a.i:64 - a.i],
                                     h_split[:, a.slot, l, k, hf * HALF:(hf + 1) * HALF],
                                     start=(a.i == 0 and k == 0 and l == 0),
                                     stop=(a.i == GB - 1 and k == KT - 1 and l == 1))
                ins.then_inc(s_cs, 1)

            PARTS = [(0, (0, 1)), (1, (0,))]

            def gemm1(a):
                pe.wait_ge(s_hlo, KT * (a.n + 1))
                for m in range(KT):
                    ge(pe, s_g, KT * (a.n - 1) + m + 1)
                    for w, ls in PARTS:
                        for k in range(KT):
                            for l in ls:
                                for hf in range(NH):
                                    ins = MM(ps1[m][:, hf], w_t[:, w, k, m * P:(m + 1) * P],
                                             h_split[:, a.slot, l, k, hf * HALF:(hf + 1) * HALF],
                                             start=(w == 0 and k == 0 and l == 0),
                                             stop=(w == 1 and k == KT - 1))
                    ins.then_inc(s_gemm1, 1)

            def gemm2(a, units):
                pe.wait_ge(s_hubset, a.n + 1)
                for u in units:
                    m, hf = divmod(u, NH)
                    ge(pe, s_o, UN * a.n + u - 1)
                    for w, ls in PARTS:
                        for k in range(KT):
                            for l in ls:
                                ins = MM(ps2[u % 2][:, :], w_t[:, w, k, m * P:(m + 1) * P],
                                         g_split[:, a.par, l, k, hf * HALF:(hf + 1) * HALF],
                                         start=(w == 0 and k == 0 and l == 0),
                                         stop=(w == 1 and k == KT - 1))
                    ins.then_inc(s_gemm2, 1)

            def matvec1(r, p):
                G = 2 * r + p
                pe.wait_ge(s_hubs, 2 * (G + 1))
                ge(pe, s_bias2, G)
                for m in range(KT):
                    for w in range(2):
                        for k in range(KT):
                            ins = MM(mv1[:, m].rearrange("p i l j -> p (i l j)"),
                                     w_t[:, w, k, m * P:(m + 1) * P],
                                     mv_in[:, k].rearrange("p i j -> p (i j)"),
                                     start=(w == 0 and k == 0), stop=(w == 1 and k == KT - 1))
                ins.then_inc(s_mv1, 1)

            def matvec2(r, p):
                G = 2 * r + p
                pe.wait_ge(s_q, G + 1)
                for m in range(KT):
                    for w in range(2):
                        for k in range(KT):
                            ins = MM(mv2[:, m].rearrange("p l i -> p (l i)"),
                                     w_t[:, w, k, m * P:(m + 1) * P],
                                     q_split[:, k].rearrange("p l i -> p (l i)"),
                                     start=(w == 0 and k == 0), stop=(w == 1 and k == KT - 1))
                ins.then_inc(s_mv2, 1)

            for d in range(LEAD):
                if d == 2:
                    pe.wait_ge(w_ready, 1)
                    gemm1(At(0, 0, 0))
                colsum(ahead(0, 0, 0, d))

            def steps(r, p):
                for i in range(GB):
                    if i or p or not isinstance(r, int) or r:
                        gemm1(At(r, p, i))
                    b = ahead(r, p, i, -1)
                    if b:
                        gemm2(b, range(NH))
                    if i == 0:
                        matvec1(r, p)
                    if b:
                        gemm2(b, range(NH, UN))
                    if b := ahead(r, p, i, LEAD):
                        colsum(b)
                    if i == 0:
                        matvec2(r, p)

            run_groups(pe, steps)
            gemm2(At(NG // 2 - 1, 1, GB - 1), range(UN))

            def any_pe(n):
                def item(e, pairs, rows=P, cols=HALF):
                    if e < BANKS:
                        pe.wait_ge(a_h, n + 1)
                    else:
                        pe.wait_ge(a_dve, ITEMS * n + (e + 1 - BANKS))
                    for z, (lhs, rhs) in enumerate(pairs):
                        ins = MM(any_bank(e)[0:rows, 0:cols], lhs, rhs, start=z == 0, stop=z == len(pairs) - 1)
                    ins.then_inc(a_pe, 1)

                def stage(e):
                    pe.wait_ge(a_dve, ITEMS * n + e)

                def products(e, src):
                    for j in range(NT):
                        item(e + j, [(src[:, k, j * P:(j + 1) * P], any_w[:, k, :]) for k in range(KT)], cols=S)

                def aggregate(e):
                    for u in range(UN):
                        m, hf = divmod(u, NH)
                        item(e + u, [(any_y[:, j, m * P:(m + 1) * P], any_adj[:, j, hf * HALF:(hf + 1) * HALF])
                                     for j in range(NT)])

                for hf in range(NH):
                    item(IT_SUM + hf, [(any_ones[:, 0:1], any_h[:, k, hf * HALF:(hf + 1) * HALF])
                                       for k in range(KT)], rows=1)
                products(IT_Y1, any_h)
                pe.wait_ge(a_rows, n + 1)
                for j in range(NT):
                    for hf in range(NH):
                        item(IT_ADJ + NH * j + hf,
                             [(a[:, j * P:(j + 1) * P], b[:, hf * HALF:(hf + 1) * HALF])
                              for a, b in ((row_some, row_hub), (row_hub, row_some),
                                           (row_zero, row_tie), (row_tie, row_zero))])
                stage(IT_DEG)
                for hf in range(NH):
                    item(IT_DEG + hf, [(any_ones, any_adj[:, j, hf * HALF:(hf + 1) * HALF]) for j in range(NT)])
                aggregate(IT_G)
                stage(IT_Y2)
                products(IT_Y2, any_g)
                stage(IT_OUT)
                aggregate(IT_OUT)

            when_flagged(pe, any_pe)


_OUT = ((32, 256, 1024), "float32")


def kernel(x, adj, L0_gnn_b1, L0_gnn_b2):
    import numpy as np
    import concourse.bacc as bacc
    from concourse.bass_utils import run_bass_kernel_spmd

    nc = bacc.Bacc("TRN2", target_bir_lowering=False, num_devices=1)
    arrays, args = {}, []
    for name, a in (("x", x), ("adj", adj), ("b1", L0_gnn_b1), ("b2", L0_gnn_b2)):
        a = np.ascontiguousarray(a)
        arrays[f"in_{name}"] = a
        args.append(nc.dram_tensor(f"in_{name}", a.shape, mybir.dt.from_np(a.dtype), kind="ExternalInput").ap())
    shape, dtype = _OUT
    o = nc.dram_tensor("out_0", shape, mybir.dt.from_np(np.dtype(dtype)), kind="ExternalOutput").ap()
    adjacency_gnn_kernel(nc, *args, o)
    r = run_bass_kernel_spmd(nc, [arrays], core_ids=[0])
    return r.results[0]["out_0"]
```
